# Optimizing a Trainium2 kernel written in Bass

```python
import numpy as np
import jax
import jax.numpy as jnp

def _softmax(x, axis=-1):
    return jax.nn.softmax(x, axis=axis)

def _gelu(x):
    return jax.nn.gelu(x, approximate=True)

def _silu(x):
    return jax.nn.silu(x)

def _sigmoid(x):
    return jax.nn.sigmoid(x)

def _layernorm(x, axis=-1, eps=1e-05):
    m = jnp.mean(x, axis=axis, keepdims=True)
    v = jnp.var(x, axis=axis, keepdims=True)
    return (x - m) / jnp.sqrt(v + eps)

def _scatter_add(tgt, idx, src, axis=0):
    return tgt.at[idx].add(src)

def _segment_sum(src, seg, n):
    return jax.ops.segment_sum(src, seg, n)
kernel_name = 'mk_dlrm_tower_d1_rec_r8_5889e6'

def setup_inputs(seed: int=0):
    np.random.seed(seed)
    _w = jnp.asarray

    def _rec_inputs():
        import jax
        import jax.numpy as jnp
        _tk = jax.random.key(seed)
        dense_ctx = jax.random.normal(jax.random.fold_in(_tk, 190), (512, 16), jnp.float32)
        ids = jnp.stack([jax.random.randint(jax.random.fold_in(_tk, 200 + f), (512,), 0, v, jnp.int32) for f, v in enumerate([1250, 1250, 12500, 1250, 12500, 1250, 12500, 1250, 1000, 12500, 125000, 1250, 1250, 12500, 12500, 125000, 1250, 1000, 1250, 125000, 1250, 1000, 1250, 12500, 1250, 1250, 1250, 1250, 1250, 1250, 1250, 1250])], axis=1)
        tbl_0 = 0.05 * jax.random.normal(jax.random.fold_in(_tk, 500 + 0), (1250, 64), jnp.float32)
        tbl_1 = 0.05 * jax.random.normal(jax.random.fold_in(_tk, 500 + 1), (1250, 64), jnp.float32)
        tbl_2 = 0.05 * jax.random.normal(jax.random.fold_in(_tk, 500 + 2), (12500, 64), jnp.float32)
        tbl_3 = 0.05 * jax.random.normal(jax.random.fold_in(_tk, 500 + 3), (1250, 64), jnp.float32)
        tbl_4 = 0.05 * jax.random.normal(jax.random.fold_in(_tk, 500 + 4), (12500, 64), jnp.float32)
        tbl_5 = 0.05 * jax.random.normal(jax.random.fold_in(_tk, 500 + 5), (1250, 64), jnp.float32)
        tbl_6 = 0.05 * jax.random.normal(jax.random.fold_in(_tk, 500 + 6), (12500, 64), jnp.float32)
        tbl_7 = 0.05 * jax.random.normal(jax.random.fold_in(_tk, 500 + 7), (1250, 64), jnp.float32)
        tbl_8 = 0.05 * jax.random.normal(jax.random.fold_in(_tk, 500 + 8), (1000, 64), jnp.float32)
        tbl_9 = 0.05 * jax.random.normal(jax.random.fold_in(_tk, 500 + 9), (12500, 64), jnp.float32)
        tbl_10 = 0.05 * jax.random.normal(jax.random.fold_in(_tk, 500 + 10), (125000, 64), jnp.float32)
        tbl_11 = 0.05 * jax.random.normal(jax.random.fold_in(_tk, 500 + 11), (1250, 64), jnp.float32)
        tbl_12 = 0.05 * jax.random.normal(jax.random.fold_in(_tk, 500 + 12), (1250, 64), jnp.float32)
        tbl_13 = 0.05 * jax.random.normal(jax.random.fold_in(_tk, 500 + 13), (12500, 64), jnp.float32)
        tbl_14 = 0.05 * jax.random.normal(jax.random.fold_in(_tk, 500 + 14), (12500, 64), jnp.float32)
        tbl_15 = 0.05 * jax.random.normal(jax.random.fold_in(_tk, 500 + 15), (125000, 64), jnp.float32)
        tbl_16 = 0.05 * jax.random.normal(jax.random.fold_in(_tk, 500 + 16), (1250, 64), jnp.float32)
        tbl_17 = 0.05 * jax.random.normal(jax.random.fold_in(_tk, 500 + 17), (1000, 64), jnp.float32)
        tbl_18 = 0.05 * jax.random.normal(jax.random.fold_in(_tk, 500 + 18), (1250, 64), jnp.float32)
        tbl_19 = 0.05 * jax.random.normal(jax.random.fold_in(_tk, 500 + 19), (125000, 64), jnp.float32)
        tbl_20 = 0.05 * jax.random.normal(jax.random.fold_in(_tk, 500 + 20), (1250, 64), jnp.float32)
        tbl_21 = 0.05 * jax.random.normal(jax.random.fold_in(_tk, 500 + 21), (1000, 64), jnp.float32)
        tbl_22 = 0.05 * jax.random.normal(jax.random.fold_in(_tk, 500 + 22), (1250, 64), jnp.float32)
        tbl_23 = 0.05 * jax.random.normal(jax.random.fold_in(_tk, 500 + 23), (12500, 64), jnp.float32)
        tbl_24 = 0.05 * jax.random.normal(jax.random.fold_in(_tk, 500 + 24), (1250, 64), jnp.float32)
        tbl_25 = 0.05 * jax.random.normal(jax.random.fold_in(_tk, 500 + 25), (1250, 64), jnp.float32)
        tbl_26 = 0.05 * jax.random.normal(jax.random.fold_in(_tk, 500 + 26), (1250, 64), jnp.float32)
        tbl_27 = 0.05 * jax.random.normal(jax.random.fold_in(_tk, 500 + 27), (1250, 64), jnp.float32)
        tbl_28 = 0.05 * jax.random.normal(jax.random.fold_in(_tk, 500 + 28), (1250, 64), jnp.float32)
        tbl_29 = 0.05 * jax.random.normal(jax.random.fold_in(_tk, 500 + 29), (1250, 64), jnp.float32)
        tbl_30 = 0.05 * jax.random.normal(jax.random.fold_in(_tk, 500 + 30), (1250, 64), jnp.float32)
        tbl_31 = 0.05 * jax.random.normal(jax.random.fold_in(_tk, 500 + 31), (1250, 64), jnp.float32)
        _rk = jax.random.fold_in(_tk, 7)
        W_top1 = 0.0606339 * jax.random.normal(jax.random.fold_in(_tk, 801), (272, 512), jnp.float32)
        W_top2 = 0.0441942 * jax.random.normal(jax.random.fold_in(_tk, 802), (512, 256), jnp.float32)
        W_top3 = 0.0625 * jax.random.normal(jax.random.fold_in(_tk, 803), (256, 1), jnp.float32)
        b_top1 = jnp.zeros((512,), jnp.float32)
        b_top2 = jnp.zeros((256,), jnp.float32)
        return (dense_ctx, ids, tbl_0, tbl_1, tbl_2, tbl_3, tbl_4, tbl_5, tbl_6, tbl_7, tbl_8, tbl_9, tbl_10, tbl_11, tbl_12, tbl_13, tbl_14, tbl_15, tbl_16, tbl_17, tbl_18, tbl_19, tbl_20, tbl_21, tbl_22, tbl_23, tbl_24, tbl_25, tbl_26, tbl_27, tbl_28, tbl_29, tbl_30, tbl_31, W_top1, b_top1, W_top2, b_top2, W_top3)
    dense_ctx, ids, tbl_0, tbl_1, tbl_2, tbl_3, tbl_4, tbl_5, tbl_6, tbl_7, tbl_8, tbl_9, tbl_10, tbl_11, tbl_12, tbl_13, tbl_14, tbl_15, tbl_16, tbl_17, tbl_18, tbl_19, tbl_20, tbl_21, tbl_22, tbl_23, tbl_24, tbl_25, tbl_26, tbl_27, tbl_28, tbl_29, tbl_30, tbl_31, W_top1, b_top1, W_top2, b_top2, W_top3 = _rec_inputs()

    def _L0_rec_setup():
        import jax, jax.numpy as jnp
        import numpy as np
        EMB_DIM = 64
        NUM_FIELDS = 32
        NUM_PAIRS = NUM_FIELDS * (NUM_FIELDS - 1) // 2
        D1 = 256
        BATCH = 256
        key = jax.random.key(seed)
        k1, k2, k3 = jax.random.split(key, 3)
        feat_emb = jax.random.normal(k1, (BATCH, NUM_FIELDS, EMB_DIM), dtype=jnp.float32)
        lim_k = float(np.sqrt(6.0 / (EMB_DIM + EMB_DIM)))
        kernel = jax.random.uniform(k2, (EMB_DIM, NUM_PAIRS, EMB_DIM), minval=-lim_k, maxval=lim_k, dtype=jnp.float32)
        lim_w = float(np.sqrt(6.0 / (NUM_PAIRS + D1)))
        W = jax.random.uniform(k3, (D1, NUM_PAIRS), minval=-lim_w, maxval=lim_w, dtype=jnp.float32)
        b = jnp.zeros((D1,), dtype=jnp.float32)
        return {'feat_emb': feat_emb, 'kernel': kernel, 'W': W, 'b': b}
    _L0_rec_all = _L0_rec_setup()
    _L0_rec_in = {k: v for k, v in _L0_rec_all.items() if k in ('kernel', 'W', 'b')}
    del _L0_rec_all
    return {'dense_ctx': dense_ctx, 'ids': ids, 'tbl_0': tbl_0, 'tbl_1': tbl_1, 'tbl_2': tbl_2, 'tbl_3': tbl_3, 'tbl_4': tbl_4, 'tbl_5': tbl_5, 'tbl_6': tbl_6, 'tbl_7': tbl_7, 'tbl_8': tbl_8, 'tbl_9': tbl_9, 'tbl_10': tbl_10, 'tbl_11': tbl_11, 'tbl_12': tbl_12, 'tbl_13': tbl_13, 'tbl_14': tbl_14, 'tbl_15': tbl_15, 'tbl_16': tbl_16, 'tbl_17': tbl_17, 'tbl_18': tbl_18, 'tbl_19': tbl_19, 'tbl_20': tbl_20, 'tbl_21': tbl_21, 'tbl_22': tbl_22, 'tbl_23': tbl_23, 'tbl_24': tbl_24, 'tbl_25': tbl_25, 'tbl_26': tbl_26, 'tbl_27': tbl_27, 'tbl_28': tbl_28, 'tbl_29': tbl_29, 'tbl_30': tbl_30, 'tbl_31': tbl_31, 'W_top1': W_top1, 'b_top1': b_top1, 'W_top2': W_top2, 'b_top2': b_top2, 'W_top3': W_top3, 'L0_rec_kernel': _L0_rec_in['kernel'], 'L0_rec_W': _L0_rec_in['W'], 'L0_rec_b': _L0_rec_in['b']}

def reference(dense_ctx, ids, tbl_0, tbl_1, tbl_2, tbl_3, tbl_4, tbl_5, tbl_6, tbl_7, tbl_8, tbl_9, tbl_10, tbl_11, tbl_12, tbl_13, tbl_14, tbl_15, tbl_16, tbl_17, tbl_18, tbl_19, tbl_20, tbl_21, tbl_22, tbl_23, tbl_24, tbl_25, tbl_26, tbl_27, tbl_28, tbl_29, tbl_30, tbl_31, W_top1, b_top1, W_top2, b_top2, W_top3, L0_rec_kernel, L0_rec_W, L0_rec_b):
    import jax
    import jax.numpy as jnp

    def _L0_rec_ref(feat_emb, kernel, W, b):
        import jax, jax.numpy as jnp
        import numpy as np
        EMB_DIM = 64
        NUM_FIELDS = 32
        NUM_PAIRS = NUM_FIELDS * (NUM_FIELDS - 1) // 2
        D1 = 256
        BATCH = 256
        num_fields = feat_emb.shape[1]
        rows, cols = np.triu_indices(num_fields, k=1)
        p = feat_emb[:, rows, :]
        q = feat_emb[:, cols, :]
        pij = jnp.einsum('bpe,dpe,bpd->bp', p, kernel, q)
        return pij @ W.T + b
    e = jnp.stack([tbl_0[ids[:, 0]], tbl_1[ids[:, 1]], tbl_2[ids[:, 2]], tbl_3[ids[:, 3]], tbl_4[ids[:, 4]], tbl_5[ids[:, 5]], tbl_6[ids[:, 6]], tbl_7[ids[:, 7]], tbl_8[ids[:, 8]], tbl_9[ids[:, 9]], tbl_10[ids[:, 10]], tbl_11[ids[:, 11]], tbl_12[ids[:, 12]], tbl_13[ids[:, 13]], tbl_14[ids[:, 14]], tbl_15[ids[:, 15]], tbl_16[ids[:, 16]], tbl_17[ids[:, 17]], tbl_18[ids[:, 18]], tbl_19[ids[:, 19]], tbl_20[ids[:, 20]], tbl_21[ids[:, 21]], tbl_22[ids[:, 22]], tbl_23[ids[:, 23]], tbl_24[ids[:, 24]], tbl_25[ids[:, 25]], tbl_26[ids[:, 26]], tbl_27[ids[:, 27]], tbl_28[ids[:, 28]], tbl_29[ids[:, 29]], tbl_30[ids[:, 30]], tbl_31[ids[:, 31]]], axis=1)
    z = _L0_rec_ref(e, L0_rec_kernel, L0_rec_W, L0_rec_b)
    z = z.reshape(z.shape[0], -1)
    h = jnp.concatenate([z, dense_ctx], axis=1)
    h = jnp.maximum(h @ W_top1 + b_top1, 0.0)
    h = jnp.maximum(h @ W_top2 + b_top2, 0.0)
    y = h @ W_top3
    return y

_drawn_inputs = setup_inputs


def setup_inputs(seed=0):
    import zlib

    import numpy as np

    out = dict(_drawn_inputs(seed))
    spreads = {'b_top1': (0.0, 0.1), 'b_top2': (0.0, 0.1), 'L0_rec_b': (0.0, 0.1)}
    factors = {'tbl_0': 3.544,
     'tbl_1': 3.084,
     'tbl_2': 3.098,
     'tbl_3': 3.146,
     'tbl_4': 3.324,
     'tbl_5': 3.166,
     'tbl_6': 3.274,
     'tbl_7': 3.158,
     'tbl_8': 3.543,
     'tbl_9': 3.114,
     'tbl_10': 3.307,
     'tbl_11': 3.13,
     'tbl_12': 3.101,
     'tbl_13': 3.432,
     'tbl_14': 3.234,
     'tbl_15': 3.398,
     'tbl_16': 3.589,
     'tbl_17': 3.242,
     'tbl_18': 3.342,
     'tbl_19': 3.062,
     'tbl_20': 3.251,
     'tbl_21': 3.523,
     'tbl_22': 3.643,
     'tbl_23': 2.97,
     'tbl_24': 3.563,
     'tbl_25': 3.021,
     'tbl_26': 3.108,
     'tbl_27': 3.375,
     'tbl_28': 3.229,
     'tbl_29': 3.384,
     'tbl_30': 3.373,
     'tbl_31': 3.405}
    for name, (base, spread) in spreads.items():
        noise = np.random.default_rng([zlib.crc32(name.encode()), seed]).standard_normal(out[name].shape)
        drawn = base * np.exp(spread * noise) if base else spread * noise
        out[name] = jnp.asarray(drawn.astype(out[name].dtype))
    for name, factor in factors.items():
        out[name] = (out[name] * factor).astype(out[name].dtype)
    return out
```

```python
from contextlib import ExitStack

import concourse.bass as bass
from concourse import mybir

F32 = mybir.dt.float32
F32R = mybir.dt.float32r
U32 = mybir.dt.uint32
ALU = mybir.AluOpType
ACT = mybir.ActivationFunctionType

P = 128
BATCH = 512
FIELDS = 32
EMB = 64
D1 = 256
CTX = 16
H1, H2 = 512, 256
BT = BATCH // P
CHUNKS = FIELDS // 2
TILES = [(c, i) for c in range(CHUNKS) for i in range(2 * c + 1)]
NT = len(TILES)
GROUPS = NT // 2
COLS = 4
SLOTS = 16
WIN = COLS * SLOTS
WINS = NT // WIN
KS = 8
SLICES = NT // KS
K_RAW = 2
K_RING = 4
K_AHEAD = 20
G_RING = 4
PROD_RING = 4


def pair_index(i, j):
    return i * FIELDS - i * (i + 1) // 2 + (j - i - 1)


def plan():
    steps, slices, chunks = [], 0, 0
    for g in range(GROUPS):
        while slices < SLICES and KS * slices <= 2 * g + K_AHEAD:
            steps.append(("split", slices))
            slices += 1
        c = TILES[2 * g + 1][0]
        ahead = c if c >= 6 else 0
        while chunks < CHUNKS and chunks <= TILES[min(NT - 1, 2 * g + 1 + ahead)][0]:
            steps.append(("fields", chunks))
            chunks += 1
        steps.append(("group", g))
    return steps


def build(nc, ids, tables, kern, w_pairs, b_int, dense_t, w1, b1, w2, b2, w3, ident, selector, out):
    steps = plan()
    with ExitStack() as ctx:
        def sb(name, shape, dt=F32):
            return ctx.enter_context(nc.sbuf_tensor(name, shape, dt))

        def sem(name):
            return ctx.enter_context(nc.semaphore(name))

        ids_sb = sb("ids_sb", [P, BT, FIELDS], U32)
        gathered = sb("gathered", [P, G_RING, BT, 2 * EMB])
        parts = sb("parts", [P, 2, BT, 2, 2 * EMB])
        x_split = sb("x_split", [P, FIELDS, BATCH], F32R)
        partner = sb("partner", [P, CHUNKS, BATCH])
        k_raw = sb("k_raw", [P, K_RAW, KS * P])
        k_hi = sb("k_hi", [P, K_RING, KS, P], F32R)
        k_lo = sb("k_lo", [P, K_RING, KS, P], F32R)
        prod = sb("prod", [P, PROD_RING, 2, BATCH])
        pair_sums = sb("pair_sums", [P, WINS, BATCH])
        ident_sb = sb("ident_sb", [P, P])
        sel_sb = sb("sel_sb", [P, 2 * 32 - 2])
        w_pairs_sb = sb("w_pairs_sb", [P, WINS, D1])
        w1_sb = sb("w1_sb", [P, 2, H1])
        w1c_sb = sb("w1c_sb", [CTX, H1])
        w2_sb = sb("w2_sb", [P, H1 // P, H2])
        w3_sb = sb("w3_sb", [P, H2 // P])
        dense_sb = sb("dense_sb", [CTX, BATCH])
        b_int_sb = sb("b_int_sb", [P, D1 // P])
        b1_sb = sb("b1_sb", [P, H1 // P])
        b2_sb = sb("b2_sb", [P, H2 // P])
        y_sb = sb("y_sb", [1, BATCH])
        h1_sb, z_sb, h2_sb = partner[:, 0:4], partner[:, 4:6], partner[:, 6:8]

        t_ps = ctx.enter_context(nc.psum_tensor("t_ps", [P, 2, 2, BATCH], F32))
        tp_ps = ctx.enter_context(nc.psum_tensor("tp_ps", [P, 2, BATCH], F32))
        sum_ps = ctx.enter_context(nc.psum_tensor("sum_ps", [P, 2, BATCH], F32))

        ids_in = sem("ids_in")
        ident_in = sem("ident_in")
        top_in = sem("top_in")
        raw_in = [sem(f"raw_in{r}") for r in range(K_RAW)]
        rows_in = [sem(f"rows_in{r}") for r in range(G_RING)]
        k_rounded = sem("k_rounded")
        k_ready = sem("k_ready")
        turned = sem("turned")
        high_ready = sem("high_ready")
        low_ready = sem("low_ready")
        turned_kept = sem("turned_kept")
        t_ready = sem("t_ready")
        prod_ready = sem("prod_ready")
        prod_used = sem("prod_used")
        window_kept = sem("window_kept")
        z_done = sem("z_done")
        z_kept = sem("z_kept")
        h1_done = sem("h1_done")
        h1_kept_a = sem("h1_kept_a")
        h1_kept_v = sem("h1_kept_v")
        h2_done = sem("h2_done")
        h2_kept_a = sem("h2_kept_a")
        h2_kept_v = sem("h2_kept_v")
        y_done = sem("y_done")
        y_kept = sem("y_kept")
        stored = sem("stored")
        block = ctx.enter_context(nc.Block())

        TOP = [(w_pairs_sb[:], w_pairs), (w1_sb[:], w1[0:D1].rearrange("(k p) n -> p k n", p=P)),
               (w1c_sb[:], w1[D1:D1 + CTX]), (w2_sb[:], w2.rearrange("(k p) n -> p k n", p=P)),
               (w3_sb[:], w3), (dense_sb[:], dense_t), (b_int_sb[:], b_int), (b1_sb[:], b1), (b2_sb[:], b2)]
        n_top = 16 * len(TOP)

        @block.sync
        def _(sp):
            sp.dma_start(ids_sb[:], ids.bitcast(U32).rearrange("(t p) f -> p t f", p=P)).then_inc(ids_in, 16)
            sp.dma_start(ident_sb[:], ident).then_inc(ident_in, 16)
            sp.dma_start(sel_sb[:], selector).then_inc(ident_in, 16)
            for s in range(SLICES):
                if s >= K_RAW:
                    sp.wait_ge(k_ready, s - K_RAW + 1)
                for half in range(2):
                    sp.dma_start(k_raw[half * EMB:(half + 1) * EMB, s % K_RAW, :],
                                 kern[:, s * KS * P:(s + 1) * KS * P]).then_inc(raw_in[s % K_RAW], 16)
                if s == K_RAW:
                    for dst, src in TOP:
                        sp.dma_start(dst, src).then_inc(top_in, 16)
            sp.wait_ge(y_kept, 1)
            sp.dma_start(out.rearrange("b a -> a b"), y_sb[:]).then_inc(stored, 16)
            sp.wait_ge(stored, 16)

        @block.gpsimd
        def _(pool):
            pool.wait_ge(ids_in, 16)
            for c in range(CHUNKS):
                if c >= G_RING:
                    pool.wait_ge(turned, 3 * (c - G_RING) + 3)
                for f in range(2):
                    for t in range(BT):
                        pool.indirect_dma_start(
                            gathered[:, c % G_RING, t, f * EMB:(f + 1) * EMB], None, tables[2 * c + f],
                            bass.IndirectOffsetOnAxis(ap=ids_sb[:, t, 2 * c + f:2 * c + f + 1], axis=0),
                        ).then_inc(rows_in[c % G_RING], 16)

        @block.tensor
        def _(pe):
            def turn_fields(c):
                if c == 0:
                    pe.wait_ge(ident_in, 32)
                pe.wait_ge(low_ready, c + 1)
                for u in range(3):
                    n = 3 * c + u
                    if n >= 2:
                        pe.wait_ge(turned_kept, n - 1)
                    for t in range(BT):
                        rows = parts[:, c % 2, t, u] if u < 2 else gathered[:, c % G_RING, t]
                        mm = pe.transpose(tp_ps[:, n % 2, t * P:(t + 1) * P], rows, ident_sb[:])
                    mm.then_inc(turned, 1)

            def products(g):
                if g >= 2:
                    pe.wait_ge(prod_ready, g - 1)
                for h in range(2):
                    t = 2 * g + h
                    c, i = TILES[t]
                    s, k = t // KS, t % KS
                    if t % KS == 0:
                        pe.wait_ge(k_ready, s + 1)
                    if i == 0 or (i == 1 and h == 0):
                        pe.wait_ge(turned_kept, 3 * c + 2)
                    pe.matmul(t_ps[:, g % 2, h, :], k_hi[:, s % K_RING, k, :], x_split[:, i, :], start=True, stop=False)
                    mm = pe.matmul(t_ps[:, g % 2, h, :], k_lo[:, s % K_RING, k, :], x_split[:, i, :],
                                   start=False, stop=True)
                mm.then_inc(t_ready, 1)

            def reduce(q):
                w, k = q // SLOTS, q % SLOTS
                pe.wait_ge(prod_ready, 2 * q + 2)
                if k == 0 and w >= 2:
                    pe.wait_ge(window_kept, w - 1)
                for j in range(COLS):
                    t = COLS * q + j
                    mm = pe.matmul(sum_ps[32 * j:32 * j + 32, w % 2, :], sel_sb[:, 30 - 2 * k:62 - 2 * k],
                                   prod[:, (t // 2) % PROD_RING, t % 2, :], start=(k == 0), stop=(k == SLOTS - 1),
                                   tile_position=(0, 32 * j))
                mm.then_inc(prod_used, 1)

            for kind, n in steps:
                if kind == "fields":
                    turn_fields(n)
                if kind == "group":
                    products(n)
                    if n % 2 == 1 and n >= 3:
                        reduce((n - 3) // 2)
            reduce(GROUPS // 2 - 1)

            pe.wait_ge(top_in, n_top)
            pe.wait_ge(window_kept, WINS)
            for m in range(D1 // P):
                for w in range(WINS):
                    mm = pe.matmul(t_ps[:, 0, m, :], w_pairs_sb[:, w, m * P:(m + 1) * P], pair_sums[:, w, :],
                                   start=(w == 0), stop=(w == WINS - 1))
                mm.then_inc(z_done, 1)
            h1_ps = [t_ps[:, 1, 0, :], t_ps[:, 1, 1, :], tp_ps[:, 0, :], tp_ps[:, 1, :]]
            for n in range(H1 // P):
                pe.matmul(h1_ps[n], w1c_sb[:, n * P:(n + 1) * P], dense_sb[:], start=True, stop=False)
                for m in range(2):
                    if n == 0:
                        pe.wait_ge(z_kept, m + 1)
                    mm = pe.matmul(h1_ps[n], w1_sb[:, m, n * P:(n + 1) * P], z_sb[:, m, :], start=False, stop=(m == 1))
                mm.then_inc(h1_done, 1)
            for n in range(H2 // P):
                for m in range(H1 // P):
                    if n == 0:
                        pe.wait_ge(h1_kept_a if m % 2 == 0 else h1_kept_v, m // 2 + 1)
                    mm = pe.matmul(sum_ps[:, n, :], w2_sb[:, m, n * P:(n + 1) * P], h1_sb[:, m, :],
                                   start=(m == 0), stop=(m == H1 // P - 1))
                mm.then_inc(h2_done, 1)
            for m in range(H2 // P):
                pe.wait_ge(h2_kept_a if m == 0 else h2_kept_v, 1)
                mm = pe.matmul(t_ps[0:1, 0, 0, :], w3_sb[:, m:m + 1], h2_sb[:, m, :], start=(m == 0),
                               stop=(m == H2 // P - 1))
            mm.then_inc(y_done, 1)

        @block.scalar
        def _(act):
            def keep_window(w):
                act.wait_ge(prod_used, SLOTS * (w + 1))
                act.copy(pair_sums[:, w, :], sum_ps[:, w % 2, :]).then_inc(window_kept, 1)

            for kind, n in steps:
                if kind == "split":
                    act.wait_ge(raw_in[n % K_RAW], 32 * (n // K_RAW + 1))
                    if n >= K_RING:
                        act.wait_ge(t_ready, (n - K_RING + 1) * KS // 2)
                    act.copy(k_hi[:, n % K_RING].rearrange("p k m -> p (k m)"), k_raw[:, n % K_RAW, :]).then_inc(k_rounded, 1)
                if kind == "fields":
                    act.wait_ge(rows_in[n % G_RING], 2 * BT * 16 * (n // G_RING + 1))
                    if n >= 2:
                        act.wait_ge(turned, 3 * (n - 2) + 2)
                    rows = gathered[:, n % G_RING].rearrange("p t (f e) -> p t f e", f=2)
                    act.copy(parts[:, n % 2, :, :, 0:EMB].bitcast(F32R), rows).then_inc(high_ready, 1)
                    for u in range(3):
                        act.wait_ge(turned, 3 * n + u + 1)
                        dst = x_split[:, 2 * n + u, :] if u < 2 else partner[:, n, :]
                        act.copy(dst, tp_ps[:, (3 * n + u) % 2, :]).then_inc(turned_kept, 1)
                if kind == "group" and n % 2 == 1 and n >= 3 and (n - 3) // 2 % SLOTS == 3 and (n - 3) // 2 >= SLOTS:
                    keep_window((n - 3) // 2 // SLOTS - 1)
            keep_window(WINS - 1)
            act.wait_ge(top_in, n_top)
            for m in range(2):
                act.wait_ge(z_done, m + 1)
                act.activation(z_sb[:, m, :], t_ps[:, 0, m, :], ACT.Identity, bias=b_int_sb[:, m:m + 1]).then_inc(z_kept, 1)
            act.wait_ge(h1_done, 1)
            act.activation(h1_sb[:, 0, :], t_ps[:, 1, 0, :], ACT.Relu, bias=b1_sb[:, 0:1]).then_inc(h1_kept_a, 1)
            act.wait_ge(h1_done, 3)
            act.activation(h1_sb[:, 2, :], tp_ps[:, 0, :], ACT.Relu, bias=b1_sb[:, 2:3]).then_inc(h1_kept_a, 1)
            act.wait_ge(h2_done, 1)
            act.activation(h2_sb[:, 0, :], sum_ps[:, 0, :], ACT.Relu, bias=b2_sb[:, 0:1]).then_inc(h2_kept_a, 1)
            act.wait_ge(y_done, 1)
            act.copy(y_sb[:], t_ps[0:1, 0, 0, :]).then_inc(y_kept, 1)

        @block.vector
        def _(dve):
            for kind, n in steps:
                if kind == "split":
                    dve.wait_ge(k_rounded, n + 1)
                    hi = k_hi[:, n % K_RING].rearrange("p k m -> p (k m)")
                    lo = k_lo[:, n % K_RING].rearrange("p k m -> p (k m)")
                    dve.tensor_tensor(lo, k_raw[:, n % K_RAW, :], hi.bitcast(F32), ALU.subtract).then_inc(k_ready, 1)
                if kind == "fields":
                    dve.wait_ge(high_ready, n + 1)
                    rows = gathered[:, n % G_RING].rearrange("p t (f e) -> p t f e", f=2)
                    dve.tensor_tensor(parts[:, n % 2, :, :, EMB:], rows, parts[:, n % 2, :, :, 0:EMB],
                                      ALU.subtract).then_inc(low_ready, 1)
                if kind == "group":
                    c0, c1 = TILES[2 * n][0], TILES[2 * n + 1][0]
                    dve.wait_ge(t_ready, n + 1)
                    if n >= PROD_RING:
                        dve.wait_ge(prod_used, (n - PROD_RING) // 2 + 1)
                    dve.wait_ge(turned_kept, 3 * c1 + 3)
                    q = partner[:, c0:c0 + 2, :] if c1 > c0 else partner[:, c0:c0 + 1, :].broadcast_to([P, 2, BATCH])
                    dve.tensor_tensor(prod[:, n % PROD_RING], t_ps[:, n % 2], q, ALU.mult).then_inc(prod_ready, 1)
            dve.wait_ge(top_in, n_top)
            dve.wait_ge(h1_done, 2)
            dve.tensor_scalar(h1_sb[:, 1, :], t_ps[:, 1, 1, :], b1_sb[:, 1:2], 0.0, ALU.add, ALU.max).then_inc(h1_kept_v, 1)
            dve.wait_ge(h1_done, 4)
            dve.tensor_scalar(h1_sb[:, 3, :], tp_ps[:, 1, :], b1_sb[:, 3:4], 0.0, ALU.add, ALU.max).then_inc(h1_kept_v, 1)
            dve.wait_ge(h2_done, 2)
            dve.tensor_scalar(h2_sb[:, 1, :], sum_ps[:, 1, :], b2_sb[:, 1:2], 0.0, ALU.add, ALU.max).then_inc(h2_kept_v, 1)


def kernel(**inputs):
    import numpy as np
    import concourse.bacc as bacc
    from concourse.bass_utils import run_bass_kernel_spmd

    kern = np.asarray(inputs["L0_rec_kernel"])
    w = np.asarray(inputs["L0_rec_W"])
    kern_tiles = np.zeros((EMB, NT, 2, EMB), kern.dtype)
    w_pairs = np.zeros((P, WINS, D1), w.dtype)
    for t, (c, i) in enumerate(TILES):
        for h in range(2):
            j = 2 * c + h
            if i < j:
                kern_tiles[:, t, h, :] = kern[:, pair_index(i, j), :].T
                q, k = t // COLS, t // COLS % SLOTS
                w_pairs[32 * (t % COLS) + 2 * k + h, q // SLOTS, :] = w[:, pair_index(i, j)]
    selector = np.zeros((P, 62), np.float32)
    selector[0:EMB, 30] = 1
    selector[EMB:P, 31] = 1
    arrays = {
        "ids": np.asarray(inputs["ids"]),
        **{f"tbl_{f}": np.asarray(inputs[f"tbl_{f}"]) for f in range(FIELDS)},
        "kern": kern_tiles.reshape(EMB, NT * P),
        "w_pairs": w_pairs,
        "b_int": np.asarray(inputs["L0_rec_b"]).reshape(-1, P).T,
        "dense_t": np.asarray(inputs["dense_ctx"]).T,
        "w1": np.asarray(inputs["W_top1"]),
        "b1": np.asarray(inputs["b_top1"]).reshape(-1, P).T,
        "w2": np.asarray(inputs["W_top2"]),
        "b2": np.asarray(inputs["b_top2"]).reshape(-1, P).T,
        "w3": np.asarray(inputs["W_top3"]).reshape(-1, P).T,
        "ident": np.eye(P, dtype=np.float32),
        "selector": selector,
    }
    nc = bacc.Bacc("TRN2", target_bir_lowering=False, num_devices=1)
    arrays = {f"in_{name}": np.ascontiguousarray(a) for name, a in arrays.items()}
    aps = {name[3:]: nc.dram_tensor(name, a.shape, mybir.dt.from_np(a.dtype), kind="ExternalInput").ap()
           for name, a in arrays.items()}
    tables = [aps.pop(f"tbl_{f}") for f in range(FIELDS)]
    out = nc.dram_tensor("out_y", (BATCH, 1), F32, kind="ExternalOutput").ap()
    build(nc, tables=tables, out=out, **aps)
    return run_bass_kernel_spmd(nc, [arrays], core_ids=[0]).results[0]["out_y"]
```

```python
from contextlib import ExitStack

import concourse.bass as bass
from concourse import mybir

F32 = mybir.dt.float32
F32R = mybir.dt.float32r
U32 = mybir.dt.uint32
ALU = mybir.AluOpType
ACT = mybir.ActivationFunctionType

P = 128
BATCH = 512
FIELDS = 32
EMB = 64
D1 = 256
CTX = 16
H1, H2 = 512, 256
BT = BATCH // P
CHUNKS = FIELDS // 2
TILES = [(c, i) for c in range(CHUNKS) for i in range(2 * c + 1)]
NT = len(TILES)
GROUPS = NT // 2
COLS = 4
SLOTS = 16
WIN = COLS * SLOTS
WINS = NT // WIN
KS = 8
SLICES = NT // KS
K_RAW = 2
K_RING = 10
POOL_FROM = 16
POOL_LEAD = 40
T_RING = 3
LEAD = 4
E_RING = 3
G_RING = 4
PROD_RING = 4


def pair_index(i, j):
    return i * FIELDS - i * (i + 1) // 2 + (j - i - 1)


def last_group(c):
    return ((c + 1) ** 2 - 1) // 2


def plan():
    steps, slices, chunks = [], 0, 0
    for g in range(GROUPS):
        room = (2 * g - KS) // KS + K_RING
        while chunks < CHUNKS and chunks * chunks - min(LEAD, max(0, 2 * chunks - 2)) <= 2 * g + 1:
            while slices < min(POOL_FROM, room, 2 + 3 * chunks):
                steps.append(("split", slices))
                slices += 1
            steps.append(("fields", chunks))
            chunks += 1
        while slices < SLICES and KS * slices <= 2 * g + 1 + KS:
            steps.append(("split", slices))
            slices += 1
        steps.append(("group", g))
        if g % 4 == 3 and slices < min(SLICES, room, max(POOL_FROM, (2 * g + POOL_LEAD) // KS)):
            steps.append(("split", slices))
            slices += 1
    return steps


def build(nc, ids, tables, kern, w_pairs, b_int, dense_t, w1, b1, w2, b2, w3, ident, selector, out):
    steps = plan()
    with ExitStack() as ctx:
        def sb(name, shape, dt=F32):
            return ctx.enter_context(nc.sbuf_tensor(name, shape, dt))

        def sem(name):
            return ctx.enter_context(nc.semaphore(name))

        ids_sb = sb("ids_sb", [P, BT, FIELDS], U32)
        gathered = sb("gathered", [P, G_RING, BT, 2 * EMB])
        x_split = sb("x_split", [P, FIELDS, BATCH], F32R)
        partner = sb("partner", [P, E_RING, BATCH])
        k_raw = sb("k_raw", [P, K_RAW, KS * P])
        k_hi = sb("k_hi", [P, K_RING, KS, P], F32R)
        k_lo = sb("k_lo", [P, K_RING, KS, P], F32R)
        prod = sb("prod", [P, PROD_RING, 2, BATCH])
        pair_sums = sb("pair_sums", [P, WINS, BATCH])
        ident_sb = sb("ident_sb", [P, P])
        sel_sb = sb("sel_sb", [P, 2 * 32 - 2])
        w_pairs_sb = sb("w_pairs_sb", [P, WINS, D1])
        w1c_sb = sb("w1c_sb", [CTX, H1])
        w1_sb = gathered[:, 0:2].rearrange("p r t n -> p (r t n)").rearrange("p (k n) -> p k n", n=H1)
        w2_sb = gathered[:, 2:4].rearrange("p r t n -> p (r t n)").rearrange("p (k n) -> p k n", n=H2)
        w3_sb = sb("w3_sb", [P, H2 // P])
        dense_sb = sb("dense_sb", [CTX, BATCH])
        b_int_sb = sb("b_int_sb", [P, D1 // P])
        b1_sb = sb("b1_sb", [P, H1 // P])
        b2_sb = sb("b2_sb", [P, H2 // P])
        y_sb = sb("y_sb", [1, BATCH])
        h1_sb = prod[:, 0:2].rearrange("p a b n -> p (a b) n")
        z_sb, h2_sb = prod[:, 2], prod[:, 3]

        t_ps = ctx.enter_context(nc.psum_tensor("t_ps", [P, T_RING, 2, BATCH], F32))
        tp_ps = ctx.enter_context(nc.psum_tensor("tp_ps", [P, BATCH], F32))
        sum_ps = ctx.enter_context(nc.psum_tensor("sum_ps", [P, BATCH], F32))

        ids_in = sem("ids_in")
        ident_in = sem("ident_in")
        top_in = sem("top_in")
        late_in = sem("late_in")
        raw_in = [sem(f"raw_in{r}") for r in range(K_RAW)]
        rows_in = [sem(f"rows_in{r}") for r in range(G_RING)]
        k_rounded = sem("k_rounded")
        k_ready_v = sem("k_ready_v")
        k_ready_p = sem("k_ready_p")

        def wait_split(engine, s):
            if s < POOL_FROM:
                engine.wait_ge(k_ready_v, s + 1)
            else:
                engine.wait_ge(k_ready_p, s - POOL_FROM + 1)

        turned = sem("turned")
        high_ready = sem("high_ready")
        low_ready = sem("low_ready")
        partner_ready = sem("partner_ready")
        t_ready = sem("t_ready")
        prod_ready = sem("prod_ready")
        prod_used = sem("prod_used")
        window_kept = sem("window_kept")
        z_done = sem("z_done")
        z_kept = sem("z_kept")
        h1_done = sem("h1_done")
        h1_kept_a = sem("h1_kept_a")
        h1_kept_v = sem("h1_kept_v")
        h2_done = sem("h2_done")
        h2_kept_a = sem("h2_kept_a")
        h2_kept_v = sem("h2_kept_v")
        y_done = sem("y_done")
        y_kept = sem("y_kept")
        stored = sem("stored")
        block = ctx.enter_context(nc.Block())

        TOP = [(w_pairs_sb[:], w_pairs), (w1c_sb[:], w1[D1:D1 + CTX]),
               (w3_sb[:], w3), (dense_sb[:], dense_t), (b_int_sb[:], b_int), (b1_sb[:], b1), (b2_sb[:], b2)]
        n_top = 16 * len(TOP)

        @block.sync
        def _(sp):
            sp.dma_start(ids_sb[:], ids.bitcast(U32).rearrange("(t p) f -> p t f", p=P)).then_inc(ids_in, 16)
            sp.dma_start(ident_sb[:], ident).then_inc(ident_in, 16)
            sp.dma_start(sel_sb[:], selector).then_inc(ident_in, 16)
            for s in range(SLICES):
                if s >= K_RAW:
                    wait_split(sp, s - K_RAW)
                for half in range(2):
                    sp.dma_start(k_raw[half * EMB:(half + 1) * EMB, s % K_RAW, :],
                                 kern[:, s * KS * P:(s + 1) * KS * P]).then_inc(raw_in[s % K_RAW], 16)
                if s == K_RAW:
                    for dst, src in TOP:
                        sp.dma_start(dst, src).then_inc(top_in, 16)
            sp.wait_ge(turned, CHUNKS)
            sp.dma_start(w1_sb, w1[0:D1].rearrange("(k p) n -> p k n", p=P)).then_inc(late_in, 16)
            sp.dma_start(w2_sb, w2.rearrange("(k p) n -> p k n", p=P)).then_inc(late_in, 16)
            sp.wait_ge(y_kept, 1)
            sp.dma_start(out.rearrange("b a -> a b"), y_sb[:]).then_inc(stored, 16)
            sp.wait_ge(stored, 16)

        @block.gpsimd
        def _(pool):
            pool.wait_ge(ids_in, 16)

            def gather(c):
                if c >= G_RING:
                    pool.wait_ge(turned, c - G_RING + 1)
                for f in range(2):
                    for t in range(BT):
                        pool.indirect_dma_start(
                            gathered[:, c % G_RING, t, f * EMB:(f + 1) * EMB], None, tables[2 * c + f],
                            bass.IndirectOffsetOnAxis(ap=ids_sb[:, t, 2 * c + f:2 * c + f + 1], axis=0),
                        ).then_inc(rows_in[c % G_RING], 16)

            for c in range(G_RING - 1):
                gather(c)
            for kind, n in steps:
                if kind == "fields" and n + G_RING - 1 < CHUNKS:
                    gather(n + G_RING - 1)
                if kind == "split" and n >= POOL_FROM:
                    pool.wait_ge(k_rounded, n + 1)
                    hi = k_hi[:, n % K_RING].rearrange("p k m -> p (k m)")
                    lo = k_lo[:, n % K_RING].rearrange("p k m -> p (k m)")
                    pool.tensor_tensor(lo, k_raw[:, n % K_RAW, :], hi.bitcast(F32), ALU.subtract).then_inc(k_ready_p, 1)

        @block.tensor
        def _(pe):
            def turn(c):
                if c == 0:
                    pe.wait_ge(ident_in, 32)
                pe.wait_ge(rows_in[c % G_RING], 2 * BT * 16 * (c // G_RING + 1))
                if c >= 1:
                    pe.wait_ge(high_ready, 2 * c)
                for t in range(BT):
                    mm = pe.transpose(tp_ps[:, t * P:(t + 1) * P], gathered[:, c % G_RING, t], ident_sb[:])
                mm.then_inc(turned, 1)

            def products(g):
                if g >= T_RING:
                    pe.wait_ge(prod_ready, g - T_RING + 1)
                for h in range(2):
                    t = 2 * g + h
                    c, i = TILES[t]
                    s, k = t // KS, t % KS
                    if t % KS == 0:
                        wait_split(pe, s)
                    if i == 0 or (i == 1 and h == 0):
                        pe.wait_ge(low_ready, 2 * c + 2)
                    pe.matmul(t_ps[:, g % T_RING, h, :], k_hi[:, s % K_RING, k, :], x_split[:, i, :], start=True, stop=False)
                    mm = pe.matmul(t_ps[:, g % T_RING, h, :], k_lo[:, s % K_RING, k, :], x_split[:, i, :],
                                   start=False, stop=True)
                mm.then_inc(t_ready, 1)

            def reduce(q):
                w, k = q // SLOTS, q % SLOTS
                pe.wait_ge(prod_ready, 2 * q + 2)
                if k == 0 and w >= 1:
                    pe.wait_ge(window_kept, w)
                for j in range(COLS):
                    t = COLS * q + j
                    mm = pe.matmul(sum_ps[32 * j:32 * j + 32, :], sel_sb[:, 30 - 2 * k:62 - 2 * k],
                                   prod[:, (t // 2) % PROD_RING, t % 2, :], start=(k == 0), stop=(k == SLOTS - 1),
                                   tile_position=(0, 32 * j))
                mm.then_inc(prod_used, 1)

            for kind, n in steps:
                if kind == "fields":
                    turn(n)
                if kind == "group":
                    products(n)
                    if n % 2 == 1 and n >= 3:
                        reduce((n - 3) // 2)
            reduce(GROUPS // 2 - 1)

            pe.wait_ge(top_in, n_top)
            pe.wait_ge(window_kept, WINS)
            for m in range(D1 // P):
                for w in range(WINS):
                    mm = pe.matmul(t_ps[:, 0, m, :], w_pairs_sb[:, w, m * P:(m + 1) * P], pair_sums[:, w, :],
                                   start=(w == 0), stop=(w == WINS - 1))
                mm.then_inc(z_done, 1)
            pe.wait_ge(late_in, 32)
            h1_ps = [t_ps[:, 1, 0, :], t_ps[:, 1, 1, :], t_ps[:, 2, 0, :], t_ps[:, 2, 1, :]]
            for n in range(H1 // P):
                pe.matmul(h1_ps[n], w1c_sb[:, n * P:(n + 1) * P], dense_sb[:], start=True, stop=False)
                for m in range(2):
                    if n == 0:
                        pe.wait_ge(z_kept, m + 1)
                    mm = pe.matmul(h1_ps[n], w1_sb[:, m, n * P:(n + 1) * P], z_sb[:, m, :], start=False, stop=(m == 1))
                mm.then_inc(h1_done, 1)
            h2_ps = [tp_ps[:], sum_ps[:]]
            for n in range(H2 // P):
                for m in range(H1 // P):
                    if n == 0:
                        pe.wait_ge(h1_kept_a if m % 2 == 0 else h1_kept_v, m // 2 + 1)
                    mm = pe.matmul(h2_ps[n], w2_sb[:, m, n * P:(n + 1) * P], h1_sb[:, m, :],
                                   start=(m == 0), stop=(m == H1 // P - 1))
                mm.then_inc(h2_done, 1)
            for m in range(H2 // P):
                pe.wait_ge(h2_kept_a if m == 0 else h2_kept_v, 1)
                mm = pe.matmul(t_ps[0:1, 0, 0, :], w3_sb[:, m:m + 1], h2_sb[:, m, :], start=(m == 0),
                               stop=(m == H2 // P - 1))
            mm.then_inc(y_done, 1)

        @block.scalar
        def _(act):
            def keep_window(w):
                act.wait_ge(prod_used, SLOTS * (w + 1))
                act.copy(pair_sums[:, w, :], sum_ps[:]).then_inc(window_kept, 1)

            for kind, n in steps:
                if kind == "split":
                    act.wait_ge(raw_in[n % K_RAW], 32 * (n // K_RAW + 1))
                    if n >= K_RING:
                        act.wait_ge(t_ready, (n - K_RING + 1) * KS // 2)
                    act.copy(k_hi[:, n % K_RING].rearrange("p k m -> p (k m)"), k_raw[:, n % K_RAW, :]).then_inc(k_rounded, 1)
                if kind == "fields":
                    act.wait_ge(turned, n + 1)
                    if n >= E_RING:
                        act.wait_ge(prod_ready, last_group(n - E_RING) + 1)
                    act.copy(partner[:, n % E_RING, :], tp_ps[:]).then_inc(partner_ready, 1)
                    for f in range(2):
                        rows = slice(f * EMB, (f + 1) * EMB)
                        act.copy(x_split[rows, 2 * n + f, :], tp_ps[rows, :]).then_inc(high_ready, 1)
                if kind == "group" and n % 2 == 1 and n >= 3 and (n - 3) // 2 % SLOTS == SLOTS - 1:
                    keep_window((n - 3) // 2 // SLOTS)
            keep_window(WINS - 1)
            act.wait_ge(top_in, n_top)
            for m in range(2):
                act.wait_ge(z_done, m + 1)
                act.activation(z_sb[:, m, :], t_ps[:, 0, m, :], ACT.Identity, bias=b_int_sb[:, m:m + 1]).then_inc(z_kept, 1)
            act.wait_ge(h1_done, 1)
            act.activation(h1_sb[:, 0, :], t_ps[:, 1, 0, :], ACT.Relu, bias=b1_sb[:, 0:1]).then_inc(h1_kept_a, 1)
            act.wait_ge(h1_done, 3)
            act.activation(h1_sb[:, 2, :], t_ps[:, 2, 0, :], ACT.Relu, bias=b1_sb[:, 2:3]).then_inc(h1_kept_a, 1)
            act.wait_ge(h2_done, 1)
            act.activation(h2_sb[:, 0, :], tp_ps[:], ACT.Relu, bias=b2_sb[:, 0:1]).then_inc(h2_kept_a, 1)
            act.wait_ge(y_done, 1)
            act.copy(y_sb[:], t_ps[0:1, 0, 0, :]).then_inc(y_kept, 1)

        @block.vector
        def _(dve):
            for kind, n in steps:
                if kind == "split" and n < POOL_FROM:
                    dve.wait_ge(k_rounded, n + 1)
                    hi = k_hi[:, n % K_RING].rearrange("p k m -> p (k m)")
                    lo = k_lo[:, n % K_RING].rearrange("p k m -> p (k m)")
                    dve.tensor_tensor(lo, k_raw[:, n % K_RAW, :], hi.bitcast(F32), ALU.subtract).then_inc(k_ready_v, 1)
                if kind == "fields":
                    for f in range(2):
                        dve.wait_ge(high_ready, 2 * n + f + 1)
                        rows, other = slice(f * EMB, (f + 1) * EMB), slice((1 - f) * EMB, (2 - f) * EMB)
                        dve.tensor_tensor(x_split[other, 2 * n + f, :], partner[rows, n % E_RING, :],
                                          x_split[rows, 2 * n + f, :].bitcast(F32), ALU.subtract).then_inc(low_ready, 1)
                if kind == "group":
                    c0, c1 = TILES[2 * n][0], TILES[2 * n + 1][0]
                    dve.wait_ge(t_ready, n + 1)
                    if n >= PROD_RING:
                        dve.wait_ge(prod_used, (n - PROD_RING) // 2 + 1)
                    dve.wait_ge(partner_ready, c1 + 1)
                    a, b = c0 % E_RING, c1 % E_RING
                    q = partner[:, a:a + 1, :].broadcast_to([P, 2, BATCH])
                    if b == a + 1:
                        q = partner[:, a:b + 1, :]
                    if b < a:
                        q = partner[:, ::-(E_RING - 1), :]
                    dve.tensor_tensor(prod[:, n % PROD_RING], t_ps[:, n % T_RING], q, ALU.mult).then_inc(prod_ready, 1)
            dve.wait_ge(top_in, n_top)
            dve.wait_ge(h1_done, 2)
            dve.tensor_scalar(h1_sb[:, 1, :], t_ps[:, 1, 1, :], b1_sb[:, 1:2], 0.0, ALU.add, ALU.max).then_inc(h1_kept_v, 1)
            dve.wait_ge(h1_done, 4)
            dve.tensor_scalar(h1_sb[:, 3, :], t_ps[:, 2, 1, :], b1_sb[:, 3:4], 0.0, ALU.add, ALU.max).then_inc(h1_kept_v, 1)
            dve.wait_ge(h2_done, 2)
            dve.tensor_scalar(h2_sb[:, 1, :], sum_ps[:], b2_sb[:, 1:2], 0.0, ALU.add, ALU.max).then_inc(h2_kept_v, 1)


def kernel(**inputs):
    import numpy as np
    import concourse.bacc as bacc
    from concourse.bass_utils import run_bass_kernel_spmd

    kern = np.asarray(inputs["L0_rec_kernel"])
    w = np.asarray(inputs["L0_rec_W"])
    kern_tiles = np.zeros((EMB, NT, 2, EMB), kern.dtype)
    w_pairs = np.zeros((P, WINS, D1), w.dtype)
    for t, (c, i) in enumerate(TILES):
        for h in range(2):
            j = 2 * c + h
            if i < j:
                kern_tiles[:, t, h, :] = kern[:, pair_index(i, j), :].T
                q, k = t // COLS, t // COLS % SLOTS
                w_pairs[32 * (t % COLS) + 2 * k + h, q // SLOTS, :] = w[:, pair_index(i, j)]
    selector = np.zeros((P, 62), np.float32)
    selector[0:EMB, 30] = 1
    selector[EMB:P, 31] = 1
    arrays = {
        "ids": np.asarray(inputs["ids"]),
        **{f"tbl_{f}": np.asarray(inputs[f"tbl_{f}"]) for f in range(FIELDS)},
        "kern": kern_tiles.reshape(EMB, NT * P),
        "w_pairs": w_pairs,
        "b_int": np.asarray(inputs["L0_rec_b"]).reshape(-1, P).T,
        "dense_t": np.asarray(inputs["dense_ctx"]).T,
        "w1": np.asarray(inputs["W_top1"]),
        "b1": np.asarray(inputs["b_top1"]).reshape(-1, P).T,
        "w2": np.asarray(inputs["W_top2"]),
        "b2": np.asarray(inputs["b_top2"]).reshape(-1, P).T,
        "w3": np.asarray(inputs["W_top3"]).reshape(-1, P).T,
        "ident": np.eye(P, dtype=np.float32),
        "selector": selector,
    }
    nc = bacc.Bacc("TRN2", target_bir_lowering=False, num_devices=1)
    arrays = {f"in_{name}": np.ascontiguousarray(a) for name, a in arrays.items()}
    aps = {name[3:]: nc.dram_tensor(name, a.shape, mybir.dt.from_np(a.dtype), kind="ExternalInput").ap()
           for name, a in arrays.items()}
    tables = [aps.pop(f"tbl_{f}") for f in range(FIELDS)]
    out = nc.dram_tensor("out_y", (BATCH, 1), F32, kind="ExternalOutput").ap()
    build(nc, tables=tables, out=out, **aps)
    return run_bass_kernel_spmd(nc, [arrays], core_ids=[0]).results[0]["out_y"]
```

```python
from contextlib import ExitStack

import concourse.bass as bass
from concourse import mybir

F32 = mybir.dt.float32
F32R = mybir.dt.float32r
U32 = mybir.dt.uint32
I32 = mybir.dt.int32
ALU = mybir.AluOpType
ACT = mybir.ActivationFunctionType

P = 128
BATCH = 512
FIELDS = 32
EMB = 64
D1 = 256
CTX = 16
H1, H2 = 512, 256
BT = BATCH // P
CHUNKS = FIELDS // 2
ONE_HOT = (0, )
V_ROWS = 125
OH_RING = 4
SET = 4
GROUP = []
for c in range(CHUNKS):
    if c % SET == SET - 1:
        GROUP.append((c, True, [[(2 * a + 1, 2 * a), (2 * a + 2, 2 * a + 3)] for a in range(c - SET + 1, c, 2)]))
    GROUP += [(c, False, [[(i, 2 * c), (i, 2 * c + 1)] for i in (i0, i0 + 1)]) for i0 in range(0, 2 * c, 2)]
GROUPS = len(GROUP)
NT = 2 * GROUPS
MATRICES = []
USED = []
for g, (_, _, tiles) in enumerate(GROUP):
    for h, ((i, _), (k, _)) in enumerate(tiles):
        MATRICES += [(2 * g + h, (0, 1), i)] if i == k else [(2 * g + h, (0, ), i), (2 * g + h, (1, ), k)]
    USED.append(len(MATRICES))
NM = len(MATRICES)
FIRST_GROUP = [min(g for g in range(GROUPS) if GROUP[g][0] == c) if c else 0 for c in range(CHUNKS)]
COLS = 4
SLOTS = 16
WIN = COLS * SLOTS
WINS = -(-NT // WIN)
KS = 8
SLICES = NM // KS
K_RAW = 3
K_RING = 8
POOL_FROM = 12
EARLY = 3
VECTOR_LEAD = 64
POOL_LEAD = 40
T_RING = 3
LEAD = 4
PLENTY = 7
LEAD_PLENTY = 8
LOW_DEFER = 1
E_RING = 3
G_RING = 4
LATE = SLICES - 8
CTX_ROWS = 96
PROD_RING = 4


def pair_index(i, j):
    return i * FIELDS - i * (i + 1) // 2 + (j - i - 1)


GATHERED = [c for c in range(CHUNKS) if c not in ONE_HOT]


def last_group(c):
    return max(g for g in range(GROUPS) if GROUP[g][0] == c)


def set_group(k):
    return [g for g in range(GROUPS) if GROUP[g][1]][k]


def groups_of(s):
    return 1 + min(g for g in range(GROUPS) if USED[g] >= (s + 1) * KS)


def plan():
    steps, pending, slices, chunk = [], [], 0, 0
    for g in range(GROUPS):
        begun = USED[g - 1] if g else 0
        room = (begun - KS) // KS + K_RING
        while chunk < CHUNKS:
            lead = min(LEAD if chunk < PLENTY else LEAD_PLENTY, max(0, 2 * chunk - 2))
            if chunk >= 2 and 2 * FIRST_GROUP[chunk] - lead > 2 * g + 1:
                break
            while slices < min(POOL_FROM, room, EARLY * (chunk - 1) if chunk >= 2 else chunk):
                steps.append(("split", slices))
                slices += 1
            steps.append(("one_hot" if chunk in ONE_HOT else "fields", chunk))
            if chunk not in ONE_HOT:
                if chunk < 2:
                    steps.append(("low", chunk))
                else:
                    pending.append((chunk, g + (LOW_DEFER if chunk >= PLENTY else 0)))
            chunk += 1
        while slices < SLICES and KS * slices < USED[g] + KS:
            steps.append(("split", slices))
            slices += 1
        for c, due in pending[:]:
            if g >= min(due, FIRST_GROUP[c]):
                steps.append(("low", c))
                pending.remove((c, due))
        steps.append(("group", g))
        lead = VECTOR_LEAD if slices < POOL_FROM else POOL_LEAD
        if g % 4 == 3 and slices < min(SLICES, room, (begun + lead) // KS):
            steps.append(("split", slices))
            slices += 1
    return steps


def build(nc, ids, ids_t, iota, pick, tables, kern, w_pairs, b_int, ctx_rows, w_ctx_rows,
          w1, b1, w2, b2, w3, ident, selector, out):
    steps = plan()
    with ExitStack() as ctx:
        def sb(name, shape, dt=F32):
            return ctx.enter_context(nc.sbuf_tensor(name, shape, dt))

        def sem(name):
            return ctx.enter_context(nc.semaphore(name))

        ids_sb = sb("ids_sb", [P, BT, FIELDS], U32)
        gathered = sb("gathered", [P, G_RING, BT, 2 * EMB])
        table_raw = sb("table_raw", [V_ROWS, 2, 10 * EMB])
        iota_sb = sb("iota_sb", list(iota.shape))
        pick_sb = sb("pick_sb", [P, 3 * EMB], F32R)
        x_split = sb("x_split", [P, FIELDS, BATCH], F32R)
        table_split = x_split[0:V_ROWS, FIELDS - OH_RING - 5:FIELDS - OH_RING].rearrange(
            "p f b -> p (f b)").rearrange("p (k r e) -> p k r e", k=2, e=2 * EMB)
        one_hot = x_split[0:V_ROWS, FIELDS - OH_RING:FIELDS]
        partner = sb("partner", [P, E_RING, BATCH])
        k_raw = sb("k_raw", [P, K_RAW, KS * P])
        k_hi = sb("k_hi", [P, K_RING, KS, P], F32R)
        k_lo = sb("k_lo", [P, K_RING, KS, P], F32R)
        prod = sb("prod", [P, PROD_RING, 2, BATCH])
        own_partner = sb("own_partner", [P, SET // 2, BATCH])
        pair_sums = sb("pair_sums", [P, WINS, BATCH])
        ids_raw, ids_f = pair_sums[0:V_ROWS, 0:2].bitcast(I32), pair_sums[0:V_ROWS, 2:4]
        ident_sb = sb("ident_sb", [P, P])
        sel_sb = sb("sel_sb", [P, 2 * 32 - 2])
        w_pairs_raw = k_raw[:, 0, :].rearrange("p (w n) -> p w n", n=D1)
        ctx_split = sb("ctx_split", [CTX_ROWS, BATCH], F32R)
        w_ctx_split = sb("w_ctx_split", [CTX_ROWS, H1], F32R)
        w1_sb = gathered[:, 0:2].rearrange("p r t n -> p (r t n)").rearrange("p (k n) -> p k n", n=H1)
        w2_sb = gathered[:, 2:4].rearrange("p r t n -> p (r t n)").rearrange("p (k n) -> p k n", n=H2)
        w3_sb = sb("w3_sb", [P, H2 // P])
        b_int_sb = sb("b_int_sb", [P, D1 // P])
        b1_sb = sb("b1_sb", [P, H1 // P])
        b2_sb = sb("b2_sb", [P, H2 // P])
        h1_sb = prod[:, 0:2].rearrange("p a b n -> p (a b) n")
        h2_sb, y_sb = prod[:, 2], prod[:, 3, 0, 0:BT]
        pick_raw = prod[:, 2, 0, 0:3 * EMB]
        ctx_raw, w_ctx_raw = prod[0:CTX_ROWS, 3, 0], prod[0:CTX_ROWS, 3, 1]

        def late(s, n):
            return [k[:, s % K_RING].rearrange("p k m -> p (k m)").rearrange("p (a n) -> p a n", n=n)
                    for k in (k_hi, k_lo)]

        w1_hi, w1_lo = late(LATE, H1)
        wp_hi, wp_lo = late(LATE + 1, D1)
        sums_hi, sums_lo = zip(*(late(LATE + 2 + k, BATCH) for k in range(2)))
        z_hi, z_lo = late(LATE + 4, BATCH)
        w2_hi, w2_lo = late(LATE + 5, H2)
        h1_hi, h1_lo = zip(*(late(LATE + 6 + k, BATCH) for k in range(2)))

        t_ps = ctx.enter_context(nc.psum_tensor("t_ps", [P, T_RING, 2, BATCH], F32))
        tp_ps = ctx.enter_context(nc.psum_tensor("tp_ps", [P, BATCH], F32))
        sum_ps = ctx.enter_context(nc.psum_tensor("sum_ps", [P, BATCH], F32))

        ids_in = sem("ids_in")
        ident_in = sem("ident_in")
        top_in = sem("top_in")
        ctx_in = sem("ctx_in")
        pick_in = sem("pick_in")
        iota_in = sem("iota_in")
        pick_ready = sem("pick_ready")
        ctx_rounded = sem("ctx_rounded")
        ctx_ready = sem("ctx_ready")
        late_rounded = sem("late_rounded")
        late_ready = sem("late_ready")
        last_rounded = sem("last_rounded")
        last_ready = sem("last_ready")
        z_rounded = sem("z_rounded")
        late_in = sem("late_in")
        raw_in = [sem(f"raw_in{r}") for r in range(K_RAW)]
        rows_in = [sem(f"rows_in{r}") for r in range(G_RING)]
        k_rounded = sem("k_rounded")
        k_ready_v = sem("k_ready_v")
        k_ready_p = sem("k_ready_p")

        def wait_split(engine, s):
            if s < POOL_FROM:
                engine.wait_ge(k_ready_v, s + 1)
            else:
                engine.wait_ge(k_ready_p, s - POOL_FROM + 1)

        turned = sem("turned")
        table_in = [sem(f"table_in{k}") for k in range(2)]
        table_rounded = sem("table_rounded")
        table_ready = sem("table_ready")
        one_hot_ready = sem("one_hot_ready")
        one_hot_used = sem("one_hot_used")
        rows_picked = sem("rows_picked")
        x_kept = sem("x_kept")

        small, before = [], 0
        for c in ONE_HOT:
            for f in range(2):
                per = tables[2 * c + f].shape[0] // V_ROWS
                small.append((2 * c + f, per, 0 if per == 10 else 10, before))
                before += per

        def small_of(c, f):
            return 2 * ONE_HOT.index(c) + f

        def load_small(engine, k):
            field, per, _, _ = small[k]
            if k >= 2:
                engine.wait_ge(table_ready, k - 1)
            engine.dma_start(table_raw[:, k % 2, 0:per * EMB],
                             tables[field].rearrange("(p r) e -> p (r e)", r=per)).then_inc(table_in[k % 2], 16)
            engine.dma_start(ids_raw[:, k % 2, :], ids_t[field:field + 1, :].broadcast_to([V_ROWS, BATCH])
                             ).then_inc(table_in[k % 2], 16)

        def wait_bank(engine, c):
            if c >= 1:
                engine.wait_ge(own_ready, c)

        def wait_x(engine, c):
            gathered_by = len([a for a in GATHERED if a <= c])
            picked_by = len([a for a in ONE_HOT if a <= c])
            if gathered_by:
                engine.wait_ge(low_ready, 2 * gathered_by)
            if picked_by:
                engine.wait_ge(x_kept, 2 * picked_by)

        high_ready = sem("high_ready")
        low_ready = sem("low_ready")
        own_ready = sem("own_ready")
        partner_ready = sem("partner_ready")
        t_ready = sem("t_ready")
        prod_ready = sem("prod_ready")
        prod_used = sem("prod_used")
        window_kept = sem("window_kept")
        z_done = sem("z_done")
        z_kept = sem("z_kept")
        h1_done = sem("h1_done")
        h1_kept_a = sem("h1_kept_a")
        h1_kept_v = sem("h1_kept_v")
        h1_rounded = sem("h1_rounded")
        h1_ready = sem("h1_ready")
        h2_done = sem("h2_done")
        h2_kept_a = sem("h2_kept_a")
        h2_kept_v = sem("h2_kept_v")
        y_done = sem("y_done")
        y_kept = sem("y_kept")
        stored = sem("stored")
        block = ctx.enter_context(nc.Block())

        TOP = [(w3_sb[:], w3), (b_int_sb[:], b_int), (b1_sb[:], b1), (b2_sb[:], b2)]
        n_top = 16 * len(TOP)

        def late_splits():
            yield w1_hi, w1_lo, w1_sb
            yield wp_hi, wp_lo, w_pairs_raw
            yield sums_hi[0], sums_lo[0], pair_sums[:, 0:2]
            yield sums_hi[1][:, 0:1], sums_lo[1][:, 0:1], pair_sums[:, 2:3]
            yield w2_hi, w2_lo, w2_sb

        @block.sync
        def _(sp):
            sp.dma_start(ids_sb[:], ids.bitcast(U32).rearrange("(t p) f -> p t f", p=P)).then_inc(ids_in, 16)
            def load_slice(s):
                if s >= K_RAW:
                    wait_split(sp, s - K_RAW)
                for half in range(2):
                    sp.dma_start(k_raw[half * EMB:(half + 1) * EMB, s % K_RAW, :],
                                 kern[:, s * KS * P:(s + 1) * KS * P]).then_inc(raw_in[s % K_RAW], 16)

            load_small(sp, 0)
            sp.dma_start(iota_sb[:], iota).then_inc(iota_in, 16)
            load_small(sp, 1)
            sp.dma_start(ident_sb[:], ident).then_inc(ident_in, 16)
            sp.dma_start(sel_sb[:], selector).then_inc(ident_in, 16)
            sp.dma_start(ctx_raw, ctx_rows).then_inc(ctx_in, 16)
            sp.dma_start(w_ctx_raw, w_ctx_rows).then_inc(ctx_in, 16)
            sp.dma_start(pick_raw, pick).then_inc(pick_in, 16)

            for s in range(SLICES):
                load_slice(s)
                if s == K_RING:
                    for dst, src in TOP:
                        sp.dma_start(dst, src).then_inc(top_in, 16)
            wait_split(sp, SLICES - 1)
            sp.dma_start(w_pairs_raw, w_pairs).then_inc(late_in, 16)
            sp.wait_ge(turned, len(GATHERED))
            sp.dma_start(w1_sb, w1[0:D1].rearrange("(k p) n -> p k n", p=P)).then_inc(late_in, 16)
            sp.dma_start(w2_sb, w2.rearrange("(k p) n -> p k n", p=P)).then_inc(late_in, 16)
            sp.wait_ge(y_kept, 1)
            sp.dma_start(out.rearrange("(p t) a -> p (t a)", t=BT), y_sb).then_inc(stored, 16)
            sp.wait_ge(stored, 16)

        @block.gpsimd
        def _(pool):
            pool.wait_ge(ids_in, 16)

            def gather(n):
                if n >= G_RING:
                    pool.wait_ge(turned, n - G_RING + 1)
                for f in range(2):
                    field = 2 * GATHERED[n] + f
                    for t in range(BT):
                        pool.indirect_dma_start(
                            gathered[:, n % G_RING, t, f * EMB:(f + 1) * EMB], None, tables[field],
                            bass.IndirectOffsetOnAxis(ap=ids_sb[:, t, field:field + 1], axis=0),
                        ).then_inc(rows_in[n % G_RING], 16)

            for n in range(G_RING - 1):
                gather(n)
            for kind, n in steps:
                if kind == "fields" and GATHERED.index(n) + G_RING - 1 < len(GATHERED):
                    gather(GATHERED.index(n) + G_RING - 1)
                if kind == "split" and n >= POOL_FROM:
                    pool.wait_ge(k_rounded, n + 1)
                    hi = k_hi[:, n % K_RING].rearrange("p k m -> p (k m)")
                    lo = k_lo[:, n % K_RING].rearrange("p k m -> p (k m)")
                    pool.tensor_tensor(lo, k_raw[:, n % K_RAW, :], hi.bitcast(F32), ALU.subtract).then_inc(k_ready_p, 1)
            for n, (hi, lo, whole) in enumerate(late_splits()):
                pool.wait_ge(late_rounded, n + 1)
                pool.tensor_tensor(lo, whole, hi.bitcast(F32), ALU.subtract).then_inc(late_ready, 1)

        @block.tensor
        def _(pe):
            def turn(c):
                n = GATHERED.index(c)
                if n == 0:
                    pe.wait_ge(ident_in, 32)
                pe.wait_ge(rows_in[n % G_RING], 2 * BT * 16 * (n // G_RING + 1))
                wait_bank(pe, c)
                for t in range(BT):
                    mm = pe.transpose(tp_ps[:, t * P:(t + 1) * P], gathered[:, n % G_RING, t], ident_sb[:])
                mm.then_inc(turned, 1)

            def pick_rows(c):
                wait_bank(pe, c)
                for f in range(2):
                    k = small_of(c, f)
                    _, per, _, first = small[k]
                    pe.wait_ge(table_ready, k + 1)
                    if f == 1:
                        pe.wait_ge(x_kept, k)
                    for r in range(per):
                        pe.wait_ge(one_hot_ready, first + r + 1)
                        pe.matmul(tp_ps[:], table_split[:, k % 2, r, :], one_hot[:, (first + r) % OH_RING, :],
                                  start=(r == 0), stop=(r == per - 1)).then_inc(one_hot_used, 1)
                pe.wait_ge(x_kept, k + 1)
                if k == 1:
                    pe.wait_ge(pick_ready, 1)
                pe.matmul(tp_ps[:], pick_sb[:, EMB:3 * EMB], x_split[:, 2 * c, :], start=True, stop=False)
                pe.matmul(tp_ps[:], pick_sb[:, 0:2 * EMB], x_split[:, 2 * c + 1, :], start=False,
                          stop=True).then_inc(rows_picked, 1)

            def products(g):
                if g >= T_RING:
                    pe.wait_ge(prod_ready, g - T_RING + 1)
                if g == FIRST_GROUP[GROUP[g][0]]:
                    wait_x(pe, GROUP[g][0])
                for m in range(USED[g - 1] if g else 0, USED[g]):
                    t, _, i = MATRICES[m]
                    s, k = m // KS, m % KS
                    if k == 0:
                        wait_split(pe, s)
                    begins = m == 0 or MATRICES[m - 1][0] != t
                    ends = m == NM - 1 or MATRICES[m + 1][0] != t
                    pe.matmul(t_ps[:, g % T_RING, t % 2, :], k_hi[:, s % K_RING, k, :], x_split[:, i, :],
                              start=begins, stop=False)
                    mm = pe.matmul(t_ps[:, g % T_RING, t % 2, :], k_lo[:, s % K_RING, k, :], x_split[:, i, :],
                                   start=False, stop=ends)
                mm.then_inc(t_ready, 1)

            def reduce(q):
                w, k = q // SLOTS, q % SLOTS
                pe.wait_ge(prod_ready, 2 * q + 2)
                if k == 0 and w >= 1:
                    pe.wait_ge(window_kept, w)
                for j in range(COLS):
                    t = COLS * q + j
                    mm = pe.matmul(sum_ps[32 * j:32 * j + 32, :], sel_sb[:, 30 - 2 * k:62 - 2 * k],
                                   prod[:, (t // 2) % PROD_RING, t % 2, :], start=(k == 0),
                                   stop=(k == SLOTS - 1 or t >= NT - COLS),
                                   tile_position=(0, 32 * j))
                mm.then_inc(prod_used, 1)

            for kind, n in steps:
                if kind == "fields":
                    turn(n)
                if kind == "one_hot":
                    pick_rows(n)
                if kind == "group":
                    products(n)
                    if n % 2 == 1 and n >= 3:
                        reduce((n - 3) // 2)

            def with_high(out, w_hi, w_lo, x_hi, start):
                pe.matmul(out, w_hi, x_hi, start=start, stop=False)
                pe.matmul(out, w_lo, x_hi, start=False, stop=False)

            z_ps = t_ps[:, (GROUPS - 3) % T_RING]

            def z_high(w):
                for m in range(D1 // P):
                    cols = slice(m * P, (m + 1) * P)
                    with_high(z_ps[:, m, :], wp_hi[:, w, cols], wp_lo[:, w, cols], sums_hi[w // 2][:, w % 2, :],
                              start=(w == 0))

            def z_low(w):
                for m in range(D1 // P):
                    mm = pe.matmul(z_ps[:, m, :], wp_hi[:, w, m * P:(m + 1) * P], sums_lo[w // 2][:, w % 2, :],
                                   start=False, stop=(w == WINS - 1))
                    if w == WINS - 1:
                        mm.then_inc(z_done, 1)

            pe.wait_ge(late_ready, 4)
            pe.wait_ge(prod_ready, GROUPS - 2)
            for w in range(WINS - 1):
                z_high(w)
                z_low(w)
            reduce(GROUPS // 2 - 1)
            h1_ps = [t_ps[:, g % T_RING, h, :] for g in (GROUPS - 2, GROUPS - 1) for h in range(2)]
            pe.wait_ge(ctx_ready, 2)
            for n in range(H1 // P):
                pe.matmul(h1_ps[n], w_ctx_split[:, n * P:(n + 1) * P], ctx_split[:], start=True, stop=False)
            pe.wait_ge(last_rounded, 1)
            z_high(WINS - 1)
            pe.wait_ge(last_ready, 1)
            z_low(WINS - 1)

            def h1_high(n, m):
                cols = slice(n * P, (n + 1) * P)
                with_high(h1_ps[n], w1_hi[:, m, cols], w1_lo[:, m, cols], z_hi[:, m, :], start=False)

            def h1_low(n, m):
                return pe.matmul(h1_ps[n], w1_hi[:, m, n * P:(n + 1) * P], z_lo[:, m, :], start=False, stop=(m == 1))

            pe.wait_ge(z_rounded, 1)
            for n in range(H1 // P):
                h1_high(n, 0)
            pe.wait_ge(z_kept, 1)
            for n in range(H1 // P):
                h1_low(n, 0)
            for n in range(H1 // P):
                pe.wait_ge(z_rounded, 2)
                h1_high(n, 1)
                pe.wait_ge(z_kept, 2)
                h1_low(n, 1).then_inc(h1_done, 1)
            h2_ps = [tp_ps[:], sum_ps[:]]
            pe.wait_ge(late_ready, 5)
            for m in range(H1 // P):
                pe.wait_ge(h1_rounded, m + 1)
                for n in range(H2 // P):
                    cols = slice(n * P, (n + 1) * P)
                    with_high(h2_ps[n], w2_hi[:, m, cols], w2_lo[:, m, cols], h1_hi[m // 2][:, m % 2, :], start=(m == 0))
                pe.wait_ge(h1_ready, m + 1)
                for n in range(H2 // P):
                    mm = pe.matmul(h2_ps[n], w2_hi[:, m, n * P:(n + 1) * P], h1_lo[m // 2][:, m % 2, :],
                                   start=False, stop=(m == H1 // P - 1))
                    if m == H1 // P - 1:
                        mm.then_inc(h2_done, 1)
            pe.wait_ge(h2_kept_a, 1)
            pe.wait_ge(h2_kept_v, 1)
            for t in range(BT):
                for m in range(H2 // P):
                    mm = pe.matmul(z_ps[:, 0, t:t + 1], h2_sb[:, m, t::BT], w3_sb[:, m:m + 1], start=(m == 0),
                                   stop=(m == H2 // P - 1))
            mm.then_inc(y_done, 1)

        @block.scalar
        def _(act):
            def keep_window(w):
                act.wait_ge(prod_used, SLOTS * (w + 1))
                act.copy(pair_sums[:, w, :], sum_ps[:]).then_inc(window_kept, 1)

            def round_small(k):
                _, per, _, _ = small[k]
                act.wait_ge(table_in[k % 2], 32 * (k // 2 + 1))
                act.copy(ids_f[:, k % 2, :], ids_raw[:, k % 2, :])
                act.copy(table_split[:, k % 2, 0:per, 0:EMB],
                         table_raw[:, k % 2, 0:per * EMB].rearrange("p (r e) -> p r e", e=EMB)
                         ).then_inc(table_rounded, 1)

            for k in range(min(2, len(small))):
                round_small(k)
            if len(small) > 2:
                load_small(act, 2)
            act.wait_ge(pick_in, 16)
            act.copy(pick_sb[:], pick_raw).then_inc(pick_ready, 1)
            act.wait_ge(ctx_in, 32)
            act.copy(ctx_split[:], ctx_raw).then_inc(ctx_rounded, 1)
            act.copy(w_ctx_split[:], w_ctx_raw).then_inc(ctx_rounded, 1)
            for kind, n in steps:
                if kind == "split":
                    act.wait_ge(raw_in[n % K_RAW], 32 * (n // K_RAW + 1))
                    if n >= K_RING:
                        act.wait_ge(t_ready, groups_of(n - K_RING))
                    act.copy(k_hi[:, n % K_RING].rearrange("p k m -> p (k m)"),
                             k_raw[:, n % K_RAW, :]).then_inc(k_rounded, 1)
                if kind == "one_hot":
                    for f in range(2):
                        k = small_of(n, f)
                        act.wait_ge(one_hot_used, small[k][3] + small[k][1])
                        act.copy(x_split[:, 2 * n + f, :], tp_ps[:]).then_inc(x_kept, 1)
                        if k + 2 < len(small):
                            round_small(k + 2)
                            if k + 3 < len(small) and k + 3 >= 3:
                                load_small(act, k + 3)
                    act.wait_ge(rows_picked, small_of(n, 1) // 2 + 1)
                if kind == "fields":
                    act.wait_ge(turned, GATHERED.index(n) + 1)
                if kind in ("fields", "one_hot"):
                    if n > E_RING:
                        act.wait_ge(prod_ready, last_group(n - E_RING) + 1)
                    act.copy(partner[:, n % E_RING, :], tp_ps[:]).then_inc(partner_ready, 1)
                if kind == "fields":
                    for f in range(2):
                        rows = slice(f * EMB, (f + 1) * EMB)
                        act.copy(x_split[rows, 2 * n + f, :], tp_ps[rows, :]).then_inc(high_ready, 1)
                if kind in ("fields", "one_hot"):
                    if n % SET == 0 and n:
                        act.wait_ge(prod_ready, set_group(n // SET - 1) + 1)
                    rows = slice(n % 2 * EMB, (n % 2 + 1) * EMB)
                    act.copy(own_partner[rows, n // 2 % 2, :], tp_ps[rows, :]).then_inc(own_ready, 1)
                if kind == "group" and n % 2 == 1 and n >= 3 and (n - 3) // 2 % SLOTS == SLOTS - 1 and n < GROUPS - 1:
                    keep_window((n - 3) // 2 // SLOTS)
                if kind == "group" and n == groups_of(LATE + 4):
                    act.wait_ge(late_in, 48)
                    act.wait_ge(top_in, n_top)
                    act.wait_ge(t_ready, groups_of(LATE + 4))
                    for hi, _, whole in list(late_splits())[:-1]:
                        act.copy(hi, whole).then_inc(late_rounded, 1)
                if kind == "group" and n == groups_of(LATE + 5) + 1:
                    act.wait_ge(t_ready, groups_of(LATE + 5))
                    act.copy(w2_hi, w2_sb).then_inc(late_rounded, 1)
            act.wait_ge(prod_used, NT // COLS)
            act.copy(sums_hi[1][:, 1, :], sum_ps[:]).then_inc(last_rounded, 1)
            for m in range(2):
                act.wait_ge(z_done, m + 1)
                act.activation(z_hi[:, m, :], t_ps[:, (GROUPS - 3) % T_RING, m, :], ACT.Identity,
                               bias=b_int_sb[:, m:m + 1]).then_inc(z_rounded, 1)
            for m in (0, 2):
                act.wait_ge(h1_done, m + 1)
                for part, kept in [(h1_hi[m // 2][:, 0, :], h1_rounded), (h1_sb[:, m, :], h1_kept_a)]:
                    act.activation(part, t_ps[:, (GROUPS - 2 + m // 2) % T_RING, m % 2, :], ACT.Relu,
                                   bias=b1_sb[:, m:m + 1]).then_inc(kept, 1)
                act.wait_ge(h1_kept_v, m // 2 + 1)
                act.copy(h1_hi[m // 2][:, 1, :], h1_sb[:, m + 1, :]).then_inc(h1_rounded, 1)
            act.wait_ge(h2_done, 1)
            act.activation(h2_sb[:, 0, :], tp_ps[:], ACT.Relu, bias=b2_sb[:, 0:1]).then_inc(h2_kept_a, 1)
            act.wait_ge(y_done, 1)
            act.copy(y_sb, t_ps[:, (GROUPS - 3) % T_RING, 0, 0:BT]).then_inc(y_kept, 1)

        @block.vector
        def _(dve):
            dve.wait_ge(iota_in, 16)
            for kind, n in steps:
                if kind == "split" and n < POOL_FROM:
                    dve.wait_ge(k_rounded, n + 1)
                    hi = k_hi[:, n % K_RING].rearrange("p k m -> p (k m)")
                    lo = k_lo[:, n % K_RING].rearrange("p k m -> p (k m)")
                    dve.tensor_tensor(lo, k_raw[:, n % K_RAW, :], hi.bitcast(F32), ALU.subtract).then_inc(k_ready_v, 1)
                if kind == "one_hot":
                    for f in range(2):
                        k = small_of(n, f)
                        _, per, column, first = small[k]
                        dve.wait_ge(table_rounded, k + 1)
                        dve.tensor_tensor(table_split[:, k % 2, 0:per, EMB:],
                                          table_raw[:, k % 2, 0:per * EMB].rearrange("p (r e) -> p r e", e=EMB),
                                          table_split[:, k % 2, 0:per, 0:EMB].bitcast(F32),
                                          ALU.subtract).then_inc(table_ready, 1)
                        for r in range(per):
                            if first + r >= OH_RING:
                                dve.wait_ge(one_hot_used, first + r - OH_RING + 1)
                            dve.tensor_scalar(one_hot[:, (first + r) % OH_RING, :], ids_f[:, k % 2, :],
                                              iota_sb[:, column + r:column + r + 1], None,
                                              ALU.is_equal).then_inc(one_hot_ready, 1)
                if kind == "low":
                    for f in range(2):
                        dve.wait_ge(high_ready, 2 * GATHERED.index(n) + f + 1)
                        rows, other = slice(f * EMB, (f + 1) * EMB), slice((1 - f) * EMB, (2 - f) * EMB)
                        dve.tensor_tensor(x_split[other, 2 * n + f, :], partner[rows, n % E_RING, :],
                                          x_split[rows, 2 * n + f, :].bitcast(F32), ALU.subtract).then_inc(low_ready, 1)
                if kind == "group":
                    if n == 0:
                        for k, (parts, raw, row) in enumerate([(ctx_split, ctx_raw, 32), (w_ctx_split, w_ctx_raw, 64)]):
                            dve.wait_ge(ctx_rounded, k + 1)
                            low = parts[row:row + CTX, :]
                            dve.tensor_tensor(low, raw[row:row + CTX, :], low.bitcast(F32),
                                              ALU.subtract).then_inc(ctx_ready, 1)
                    dve.wait_ge(t_ready, n + 1)
                    if n >= PROD_RING:
                        dve.wait_ge(prod_used, (n - PROD_RING) // 2 + 1)
                    c, within, _ = GROUP[n]
                    dve.wait_ge(partner_ready, c + 1)
                    if within:
                        dve.wait_ge(own_ready, c + 1)
                    q = own_partner[:] if within else partner[:, c % E_RING:c % E_RING + 1, :].broadcast_to([P, 2, BATCH])
                    dve.tensor_tensor(prod[:, n % PROD_RING], t_ps[:, n % T_RING], q, ALU.mult).then_inc(prod_ready, 1)
            dve.wait_ge(last_rounded, 1)
            dve.tensor_tensor(sums_lo[1][:, 1, :], sum_ps[:], sums_hi[1][:, 1, :].bitcast(F32),
                              ALU.subtract).then_inc(last_ready, 1)
            dve.wait_ge(top_in, n_top)
            for m in range(2):
                dve.wait_ge(z_rounded, m + 1)
                dve.scalar_tensor_tensor(out=z_lo[:, m, :], in0=t_ps[:, (GROUPS - 3) % T_RING, m, :],
                                         scalar=b_int_sb[:, m:m + 1], in1=z_hi[:, m, :].bitcast(F32), op0=ALU.add,
                                         op1=ALU.subtract).then_inc(z_kept, 1)
            for m in (1, 3):
                dve.wait_ge(h1_done, m + 1)
                dve.tensor_scalar(h1_sb[:, m, :], t_ps[:, (GROUPS - 2 + m // 2) % T_RING, m % 2, :], b1_sb[:, m:m + 1],
                                  0.0, ALU.add, ALU.max).then_inc(h1_kept_v, 1)
                for k in (m - 1, m):
                    dve.wait_ge(h1_rounded, k + 1)
                    if k % 2 == 0:
                        dve.wait_ge(h1_kept_a, k // 2 + 1)
                    dve.tensor_tensor(h1_lo[k // 2][:, k % 2, :], h1_sb[:, k, :], h1_hi[k // 2][:, k % 2, :].bitcast(F32),
                                      ALU.subtract).then_inc(h1_ready, 1)
            dve.wait_ge(h2_done, 2)
            dve.tensor_scalar(h2_sb[:, 1, :], sum_ps[:], b2_sb[:, 1:2], 0.0, ALU.add, ALU.max).then_inc(h2_kept_v, 1)


def kernel(**inputs):
    import numpy as np
    import concourse.bacc as bacc
    from concourse.bass_utils import run_bass_kernel_spmd

    kern = np.asarray(inputs["L0_rec_kernel"])
    w = np.asarray(inputs["L0_rec_W"])
    matrices = np.zeros((EMB, NM, 2, EMB), kern.dtype)
    for m, (t, halves, i) in enumerate(MATRICES):
        for h in halves:
            _, j = GROUP[t // 2][2][t % 2][h]
            pair = pair_index(min(i, j), max(i, j))
            matrices[:, m, h, :] = kern[:, pair, :].T if i < j else kern[:, pair, :]
    w_pairs = np.zeros((P, WINS, D1), w.dtype)
    for t in range(NT):
        for h in range(2):
            i, j = sorted(GROUP[t // 2][2][t % 2][h])
            q, k = t // COLS, t // COLS % SLOTS
            w_pairs[32 * (t % COLS) + 2 * k + h, q // SLOTS, :] = w[:, pair_index(i, j)]

    def three_times(rows):
        out = np.zeros((CTX_ROWS, rows.shape[1]), rows.dtype)
        for k in range(3):
            out[32 * k:32 * k + CTX] = rows
        return out

    selector = np.zeros((P, 62), np.float32)
    selector[0:EMB, 30] = 1
    selector[EMB:P, 31] = 1
    row_numbers = [np.arange(V_ROWS)[:, None] * per + np.arange(per) for per in (10, 8)]
    pick = np.zeros((P, 3 * EMB), np.float32)
    pick[np.arange(P), EMB + np.arange(P) % EMB] = 1
    arrays = {
        "ids_t": np.asarray(inputs["ids"]).T,
        "iota": np.concatenate(row_numbers, axis=1).astype(np.float32),
        "pick": pick,
        "ids": np.asarray(inputs["ids"]),
        **{f"tbl_{f}": np.asarray(inputs[f"tbl_{f}"]) for f in range(FIELDS)},
        "kern": matrices.reshape(EMB, NM * P),
        "w_pairs": w_pairs,
        "b_int": np.asarray(inputs["L0_rec_b"]).reshape(-1, P).T,
        "ctx_rows": three_times(np.asarray(inputs["dense_ctx"]).T),
        "w_ctx_rows": three_times(np.asarray(inputs["W_top1"])[D1:]),
        "w1": np.asarray(inputs["W_top1"]),
        "b1": np.asarray(inputs["b_top1"]).reshape(-1, P).T,
        "w2": np.asarray(inputs["W_top2"]),
        "b2": np.asarray(inputs["b_top2"]).reshape(-1, P).T,
        "w3": np.asarray(inputs["W_top3"]).reshape(-1, P).T,
        "ident": np.eye(P, dtype=np.float32),
        "selector": selector,
    }
    nc = bacc.Bacc("TRN2", target_bir_lowering=False, num_devices=1)
    arrays = {f"in_{name}": np.ascontiguousarray(a) for name, a in arrays.items()}
    aps = {name[3:]: nc.dram_tensor(name, a.shape, mybir.dt.from_np(a.dtype), kind="ExternalInput").ap()
           for name, a in arrays.items()}
    tables = [aps.pop(f"tbl_{f}") for f in range(FIELDS)]
    out = nc.dram_tensor("out_y", (BATCH, 1), F32, kind="ExternalOutput").ap()
    build(nc, tables=tables, out=out, **aps)
    return run_bass_kernel_spmd(nc, [arrays], core_ids=[0]).results[0]["out_y"]
```
